# Optimizing a Trainium2 kernel written in Bass

```python
import numpy as np
import jax
import jax.numpy as jnp

def _softmax(x, axis=-1):
    return jax.nn.softmax(x, axis=axis)

def _gelu(x):
    return jax.nn.gelu(x, approximate=True)

def _silu(x):
    return jax.nn.silu(x)

def _sigmoid(x):
    return jax.nn.sigmoid(x)

def _layernorm(x, axis=-1, eps=1e-05):
    m = jnp.mean(x, axis=axis, keepdims=True)
    v = jnp.var(x, axis=axis, keepdims=True)
    return (x - m) / jnp.sqrt(v + eps)

def _scatter_add(tgt, idx, src, axis=0):
    return tgt.at[idx].add(src)

def _segment_sum(src, seg, n):
    return jax.ops.segment_sum(src, seg, n)
kernel_name = 'mk_seq_postln_d1_jaxref_r8_28d36d'

def setup_inputs(seed: int=0):
    np.random.seed(seed)
    _w = jnp.asarray

    def _L0_attn_setup():
        import jax, jax.numpy as jnp
        import numpy as np
        N, L, D, A, F, B = (4, 512, 128, 128, 512, 8)
        EPS_LN = 1e-06
        EPS_Z = 1e-06

        def _layernorm(x, scale, bias):
            m = jnp.mean(x, axis=-1, keepdims=True)
            v = jnp.mean(jnp.square(x - m), axis=-1, keepdims=True)
            return (x - m) * jax.lax.rsqrt(v + EPS_LN) * scale + bias

        def _block(x, p):
            Wq, bq, Wk, bk, Wv, bv, Wo, bo, ln1_s, ln1_b, Wf1, bf1, Wf2, bf2, ln2_s, ln2_b = p
            residual = x
            q = jnp.einsum('nld,da->nla', x, Wq) + bq
            k = jnp.einsum('nld,da->nla', x, Wk) + bk
            v = jnp.einsum('nld,da->nla', x, Wv) + bv
            Q = jax.nn.elu(q) + 1.0
            K = jax.nn.elu(k) + 1.0
            KV = jnp.einsum('nsh,nsh->nh', K, v)
            Ksum = jnp.sum(K, axis=1)
            Z = 1.0 / (Q * Ksum[:, None, :] + EPS_Z)
            V = Q * KV[:, None, :] * Z
            attn = jax.nn.gelu(jnp.einsum('nla,ad->nld', V, Wo) + bo)
            x = _layernorm(attn + residual, ln1_s, ln1_b)
            residual = x
            h = jax.nn.gelu(jnp.einsum('nld,df->nlf', x, Wf1) + bf1)
            ff = jax.nn.gelu(jnp.einsum('nlf,fd->nld', h, Wf2) + bf2)
            x = _layernorm(ff + residual, ln2_s, ln2_b)
            return (x, None)
        key = jax.random.key(seed)
        ks = jax.random.split(key, 10)
        s = 0.02
        x = jax.random.normal(ks[0], (N, L, D), dtype=jnp.float32)
        Wq = jax.random.normal(ks[1], (B, D, A), dtype=jnp.float32) * s
        Wk = jax.random.normal(ks[2], (B, D, A), dtype=jnp.float32) * s
        Wv = jax.random.normal(ks[3], (B, D, A), dtype=jnp.float32) * s
        Wo = jax.random.normal(ks[4], (B, A, D), dtype=jnp.float32) * s
        Wf1 = jax.random.normal(ks[5], (B, D, F), dtype=jnp.float32) * s
        Wf2 = jax.random.normal(ks[6], (B, F, D), dtype=jnp.float32) * s
        return {'x': x, 'Wq': Wq, 'bq': jnp.zeros((B, A), jnp.float32), 'Wk': Wk, 'bk': jnp.zeros((B, A), jnp.float32), 'Wv': Wv, 'bv': jnp.zeros((B, A), jnp.float32), 'Wo': Wo, 'bo': jnp.zeros((B, D), jnp.float32), 'ln1_s': jnp.ones((B, D), jnp.float32), 'ln1_b': jnp.zeros((B, D), jnp.float32), 'Wf1': Wf1, 'bf1': jnp.zeros((B, F), jnp.float32), 'Wf2': Wf2, 'bf2': jnp.zeros((B, D), jnp.float32), 'ln2_s': jnp.ones((B, D), jnp.float32), 'ln2_b': jnp.zeros((B, D), jnp.float32)}
    _L0_attn_in = _L0_attn_setup()

    def _L0_ffn_setup():
        import jax, jax.numpy as jnp
        import numpy as np
        EPS_LN = 1e-05
        EPS_GATE = 1e-08

        def layer_norm(x, gamma, beta):
            mu = jnp.mean(x, axis=-1, keepdims=True)
            var = jnp.mean(jnp.square(x - mu), axis=-1, keepdims=True)
            return (x - mu) * jax.lax.rsqrt(var + EPS_LN) * gamma + beta
        key = jax.random.key(seed)
        ks = jax.random.split(key, 8)
        B, S, D, E, H = (4, 512, 128, 4, 256)
        s_in = 1.0 / np.sqrt(D)
        s_h = 1.0 / np.sqrt(H)
        return {'h': jax.random.normal(ks[0], (B, S, D), dtype=jnp.float32), 'router_w': jax.random.uniform(ks[1], (E, D), jnp.float32, -s_in, s_in), 'rn_g': jnp.ones((D,), jnp.float32), 'rn_b': jnp.zeros((D,), jnp.float32), 'w1': jax.random.uniform(ks[2], (E, D, H), jnp.float32, -s_in, s_in), 'ln_g': jnp.ones((E, H), jnp.float32), 'ln_b': jnp.zeros((E, H), jnp.float32), 'w2': jax.random.uniform(ks[3], (E, H, D), jnp.float32, -s_h, s_h), 'on_g': jnp.ones((D,), jnp.float32), 'on_b': jnp.zeros((D,), jnp.float32)}
    _L0_ffn_in = _L0_ffn_setup()
    _d = {'L0_attn_x': _L0_attn_in['x'], 'L0_attn_Wq': _L0_attn_in['Wq'], 'L0_attn_bq': _L0_attn_in['bq'], 'L0_attn_Wk': _L0_attn_in['Wk'], 'L0_attn_bk': _L0_attn_in['bk'], 'L0_attn_Wv': _L0_attn_in['Wv'], 'L0_attn_bv': _L0_attn_in['bv'], 'L0_attn_Wo': _L0_attn_in['Wo'], 'L0_attn_bo': _L0_attn_in['bo'], 'L0_attn_ln1_s': _L0_attn_in['ln1_s'], 'L0_attn_ln1_b': _L0_attn_in['ln1_b'], 'L0_attn_Wf1': _L0_attn_in['Wf1'], 'L0_attn_bf1': _L0_attn_in['bf1'], 'L0_attn_Wf2': _L0_attn_in['Wf2'], 'L0_attn_bf2': _L0_attn_in['bf2'], 'L0_attn_ln2_s': _L0_attn_in['ln2_s'], 'L0_attn_ln2_b': _L0_attn_in['ln2_b'], 'L0_ffn_router_w': _L0_ffn_in['router_w'], 'L0_ffn_rn_g': _L0_ffn_in['rn_g'], 'L0_ffn_rn_b': _L0_ffn_in['rn_b'], 'L0_ffn_w1': _L0_ffn_in['w1'], 'L0_ffn_ln_g': _L0_ffn_in['ln_g'], 'L0_ffn_ln_b': _L0_ffn_in['ln_b'], 'L0_ffn_w2': _L0_ffn_in['w2'], 'L0_ffn_on_g': _L0_ffn_in['on_g'], 'L0_ffn_on_b': _L0_ffn_in['on_b']}
    _x0 = _d['L0_attn_x']
    _d['L0_attn_x'] = jax.random.normal(jax.random.fold_in(jax.random.key(seed), 1), (2, 2048, 128), dtype=_x0.dtype)
    del _x0
    return _d

def reference(L0_attn_x, L0_attn_Wq, L0_attn_bq, L0_attn_Wk, L0_attn_bk, L0_attn_Wv, L0_attn_bv, L0_attn_Wo, L0_attn_bo, L0_attn_ln1_s, L0_attn_ln1_b, L0_attn_Wf1, L0_attn_bf1, L0_attn_Wf2, L0_attn_bf2, L0_attn_ln2_s, L0_attn_ln2_b, L0_ffn_router_w, L0_ffn_rn_g, L0_ffn_rn_b, L0_ffn_w1, L0_ffn_ln_g, L0_ffn_ln_b, L0_ffn_w2, L0_ffn_on_g, L0_ffn_on_b):

    def _L0_attn_ref(x, Wq, bq, Wk, bk, Wv, bv, Wo, bo, ln1_s, ln1_b, Wf1, bf1, Wf2, bf2, ln2_s, ln2_b):
        import jax, jax.numpy as jnp
        import numpy as np
        N, L, D, A, F, B = (4, 512, 128, 128, 512, 8)
        EPS_LN = 1e-06
        EPS_Z = 1e-06

        def _layernorm(x, scale, bias):
            m = jnp.mean(x, axis=-1, keepdims=True)
            v = jnp.mean(jnp.square(x - m), axis=-1, keepdims=True)
            return (x - m) * jax.lax.rsqrt(v + EPS_LN) * scale + bias

        def _block(x, p):
            Wq, bq, Wk, bk, Wv, bv, Wo, bo, ln1_s, ln1_b, Wf1, bf1, Wf2, bf2, ln2_s, ln2_b = p
            residual = x
            q = jnp.einsum('nld,da->nla', x, Wq) + bq
            k = jnp.einsum('nld,da->nla', x, Wk) + bk
            v = jnp.einsum('nld,da->nla', x, Wv) + bv
            Q = jax.nn.elu(q) + 1.0
            K = jax.nn.elu(k) + 1.0
            KV = jnp.einsum('nsh,nsh->nh', K, v)
            Ksum = jnp.sum(K, axis=1)
            Z = 1.0 / (Q * Ksum[:, None, :] + EPS_Z)
            V = Q * KV[:, None, :] * Z
            attn = jax.nn.gelu(jnp.einsum('nla,ad->nld', V, Wo) + bo)
            x = _layernorm(attn + residual, ln1_s, ln1_b)
            residual = x
            h = jax.nn.gelu(jnp.einsum('nld,df->nlf', x, Wf1) + bf1)
            ff = jax.nn.gelu(jnp.einsum('nlf,fd->nld', h, Wf2) + bf2)
            x = _layernorm(ff + residual, ln2_s, ln2_b)
            return (x, None)
        params = (Wq, bq, Wk, bk, Wv, bv, Wo, bo, ln1_s, ln1_b, Wf1, bf1, Wf2, bf2, ln2_s, ln2_b)
        out, _ = jax.lax.scan(_block, x, params)
        return out

    def _L0_ffn_ref(h, router_w, rn_g, rn_b, w1, ln_g, ln_b, w2, on_g, on_b):
        import jax, jax.numpy as jnp
        import numpy as np
        EPS_LN = 1e-05
        EPS_GATE = 1e-08

        def layer_norm(x, gamma, beta):
            mu = jnp.mean(x, axis=-1, keepdims=True)
            var = jnp.mean(jnp.square(x - mu), axis=-1, keepdims=True)
            return (x - mu) * jax.lax.rsqrt(var + EPS_LN) * gamma + beta
        D = h.shape[-1]
        h_norm = layer_norm(h, rn_g, rn_b)
        g = jax.nn.softmax(jnp.einsum('bsd,ed->bse', h_norm, router_w), axis=-1)
        top2_w, top2_idx = jax.lax.top_k(g, 2)
        top2_w = top2_w / (jnp.sum(top2_w, axis=-1, keepdims=True) + EPS_GATE)
        hid = jnp.einsum('bsd,edh->bseh', h, w1)
        hid = jax.nn.relu(layer_norm(hid, ln_g, ln_b))
        expert_out = jnp.einsum('bseh,ehd->bsed', hid, w2)
        idx = jnp.broadcast_to(top2_idx[..., None], top2_idx.shape + (D,))
        top2_out = jnp.take_along_axis(expert_out, idx, axis=-2)
        out = jnp.sum(top2_out * top2_w[..., None], axis=-2)
        return layer_norm(out, on_g, on_b)
    x = L0_attn_x
    x = _layernorm(x + _L0_attn_ref(x, L0_attn_Wq, L0_attn_bq, L0_attn_Wk, L0_attn_bk, L0_attn_Wv, L0_attn_bv, L0_attn_Wo, L0_attn_bo, L0_attn_ln1_s, L0_attn_ln1_b, L0_attn_Wf1, L0_attn_bf1, L0_attn_Wf2, L0_attn_bf2, L0_attn_ln2_s, L0_attn_ln2_b), axis=-1)
    x = _layernorm(x + _L0_ffn_ref(x, L0_ffn_router_w, L0_ffn_rn_g, L0_ffn_rn_b, L0_ffn_w1, L0_ffn_ln_g, L0_ffn_ln_b, L0_ffn_w2, L0_ffn_on_g, L0_ffn_on_b), axis=-1)
    return x

_drawn_inputs = setup_inputs


def setup_inputs(seed=0):
    import zlib

    import numpy as np

    out = dict(_drawn_inputs(seed))
    spreads = {'L0_attn_bq': (0.0, 2.0),
     'L0_attn_bk': (0.0, 2.0),
     'L0_attn_bv': (0.0, 0.1),
     'L0_attn_bo': (0.0, 0.1),
     'L0_attn_ln1_s': (1.0, 0.2),
     'L0_attn_ln1_b': (0.0, 0.1),
     'L0_attn_bf1': (0.0, 0.1),
     'L0_attn_bf2': (0.0, 0.1),
     'L0_attn_ln2_s': (1.0, 0.2),
     'L0_attn_ln2_b': (0.0, 0.1),
     'L0_ffn_rn_g': (1.0, 0.2),
     'L0_ffn_rn_b': (0.0, 0.1),
     'L0_ffn_ln_g': (1.0, 0.2),
     'L0_ffn_ln_b': (0.0, 0.1),
     'L0_ffn_on_g': (1.0, 0.2),
     'L0_ffn_on_b': (0.0, 0.1)}
    factors = {'L0_attn_Wq': 64.0, 'L0_attn_Wk': 13.079}
    for name, (base, spread) in spreads.items():
        noise = np.random.default_rng([zlib.crc32(name.encode()), seed]).standard_normal(out[name].shape)
        drawn = base * np.exp(spread * noise) if base else spread * noise
        out[name] = jnp.asarray(drawn.astype(out[name].dtype))
    for name, factor in factors.items():
        out[name] = (out[name] * factor).astype(out[name].dtype)
    return out
```

```python
import itertools
from contextlib import ExitStack

import concourse.bass as bass
from concourse import mybir

P = 128
CH = 512
TILES = CH // P
LAYERS = 8
UNITS = 4 * LAYERS
FB = 4
NPAR = 9 + FB
BQ, BK, BV, BO, S1, B1, S2, B2, BF2, BF1 = range(10)
WCOLS = (4 + 2 * FB) * P
QKV = 3 * P
WO = QKV
WF1 = WO + P
WF2 = WF1 + FB * P
CHUNKS = 8
EXPERTS = 4
H = 256
HB = 2 * EXPERTS
EW = EXPERTS * H
LOW = 32
EPS_LN = 1e-6
EPS_OUT = 1e-5
EPS_GATE = 1e-8
TE = TILES * EXPERTS
EPS_Z = 1e-6

ALU = mybir.AluOpType
ACT = mybir.ActivationFunctionType
F32 = mybir.dt.float32
F32R = mybir.dt.float32r
AX = mybir.AxisListType
GELU = ACT.Gelu_apprx_tanh


def build(nc, x_in, w_in, par_in, const_in, w1_in, w2_in, moe_in, row_in, out):
    with ExitStack() as ctx:
        def sb(name, shape, dt=F32):
            return ctx.enter_context(nc.sbuf_tensor(name, shape, dt))

        def sem(name):
            return ctx.enter_context(nc.semaphore(name))

        x = sb("x", [P, 8 * CH])
        xr_h = sb("xr_h", [P, 4 * CH], F32R)
        xr_l = sb("xr_l", [P, 4 * CH], F32R)
        x1 = sb("x1", [P, 4 * CH])
        x1_h = sb("x1_h", [P, 4 * CH], F32R)
        x1_l = sb("x1_l", [P, 4 * CH], F32R)
        Q = sb("Q", [P, 8 * CH])
        expk = sb("expk", [P, 2 * CH])
        expq = sb("expq", [P, 2 * CH])
        reluq = sb("reluq", [P, 2 * CH])
        Kt = sb("Kt", [P, 2 * CH])
        rz = sb("rz", [P, 2 * CH])
        V = sb("V", [P, 2 * CH])
        y = [sb(f"y{n}", [P, 2 * CH]) for n in (1, 2)]
        y_h = sb("y_h", [P, 2 * CH], F32R)
        y_l = sb("y_l", [P, 2 * CH], F32R)
        cs = [sb(f"cs{n}", [P, 2 * CH]) for n in (1, 2)]
        sq = sb("sq", [P, 2 * CH])
        hid = sb("hid", [P, 2 * FB * CH])
        wraw = sb("wraw", [P, LAYERS * WCOLS + QKV])
        wqkv_h = sb("wqkv_h", [P, QKV], F32R)
        wqkv_l = sb("wqkv_l", [P, QKV], F32R)
        wo = sb("wo", [P, P])
        wf1_h = sb("wf1_h", [P, FB * P], F32R)
        wf1_l = sb("wf1_l", [P, FB * P], F32R)
        wf2 = sb("wf2", [P, FB * P])
        par = sb("par", [P, LAYERS * NPAR + 2])
        bias1 = sb("bias1", [P, LAYERS * NPAR])
        consts = sb("consts", [P, 2 * P])
        cen = sb("cen", [P, P], F32R)
        sel = sb("sel", [LOW + 2 * TILES, 2 * TILES * P], F32R)
        bias_qk = sb("bias_qk", [P, 2])
        bias_o = sb("bias_o", [P, 1])
        bias_f = sb("bias_f", [P, 1 + FB])
        mean1 = sb("mean1", [P, 1])
        epsz = sb("epsz", [P, 1])
        mhalf = sb("mhalf", [P, 2 * TILES])
        ksp = sb("ksp", [P, 8])
        kvp = sb("kvp", [P, 8])
        ks = sb("ks", [P, 2])
        kv = sb("kv", [P, 2])
        ve = [sb(f"ve{n}", [P, 2 * TILES]) for n in (1, 2)]
        rs = [sb(f"rs{n}", [P, 2 * TILES]) for n in (1, 2)]
        rs_hl = sb("rs_hl", [LOW + 2 * TILES, P], F32R)
        ident = consts[:, 0:P]

        def raw_part(at, n):
            return wraw[:, at:at + n]
        w1 = raw_part(0, EW)
        g_all = raw_part(EW, EW)
        w1c = raw_part(2 * EW, EW)
        w1ct = raw_part(3 * EW, EW)
        w2 = raw_part(4 * EW, EW)
        b_raw = raw_part(5 * EW, EW)[0:3 * EXPERTS, :]
        b_part = raw_part(6 * EW, EW)[0:3 * EXPERTS, :]
        on_g = raw_part(7 * EW, P)
        on_b = raw_part(7 * EW + P, P)
        w1_h, w1_l = xr_h[:, 0:EW], xr_l[:, 0:EW]
        gram_h, gram_l = xr_h[:, EW:EW + CH], xr_l[:, EW:EW + CH]
        b_h = x1_h[0:3 * EXPERTS, EW:2 * EW]
        b_rows = x1_l[0:3 * EXPERTS, EW:2 * EW]
        x0 = Q
        z = y[0]
        xt = x1[:, 0:2 * CH]
        xe_h, xe_l = x1_h[:, 0:2 * CH], x1_l[:, 0:2 * CH]
        std_rows = y_h[0:3 * EXPERTS, 0:CH]
        mix = V
        xb = cs[0]
        result = sq
        unused = Kt
        at = [0]

        def small(n):
            at[0] += n
            return rz[:, at[0] - n:at[0]]
        moe_small = sb("moe_small", [P, 2 + EXPERTS])
        masks = sb("masks", [P, 2 * EXPERTS * EXPERTS + 2 * EXPERTS])
        rw = small(EXPERTS)
        rw_h = sb("rw_h", [P, EXPERTS], F32R)
        rw_l = sb("rw_l", [P, EXPERTS], F32R)
        rn_b_all = small(P)
        router_b = small(EXPERTS)
        w1_mean = small(EXPERTS)
        moe_eps = sb("moe_eps", [P, 1])
        stats = [small(6 * TILES) for _ in range(3)]
        mean = [small(TILES) for _ in range(3)]
        apart = [small(TILES) for _ in range(3)]
        var = [small(TILES) for _ in range(3)]
        var_eps = [small(TILES) for _ in range(3)]
        rstd = [small(TILES) for _ in range(3)]
        minus_mean = [small(TILES) for _ in range(3)]
        x_var = small(2 * TILES)
        x_rstd = small(2 * TILES)
        hid_var = small(TE)
        hid_std = small(2 * TE)
        std_h = sb("std_h", [P, TE], F32R)
        std_parts = small(3 * TE)
        logits = small(TE)
        exps = small(TE)
        prob = small(TE)
        tile_sum = small(TILES)
        tile_rec = small(TILES)
        not_less = small(TE * EXPERTS)
        greater = small(TE * EXPERTS)
        rank = small(TE)
        top2 = small(TE)
        gate = small(2 * TE)

        R = [ctx.enter_context(nc.psum_tensor(f"R{n}", [P, CH], F32)) for n in range(3)]
        O = [ctx.enter_context(nc.psum_tensor(f"O{h}", [P, CH], F32)) for h in "ab"]
        C = ctx.enter_context(nc.psum_tensor("C", [P, CH], F32))
        L = [ctx.enter_context(nc.psum_tensor(f"L{h}", [P, CH], F32)) for h in "ab"]

        K_BANK = (R[0], O[0])
        Q_BANK = (R[2], O[1])
        V_BANK = R[1]
        HIDDEN = (R[0], R[2], R[1])

        x_loaded = [sem(f"x_loaded{c}") for c in range(8)]
        par_loaded = sem("par_loaded")
        wfirst_loaded = sem("wfirst_loaded")
        wrest_loaded = sem("wrest_loaded")
        consts_set = sem("consts_set")
        wqkv_high = sem("wqkv_high")
        wqkv_set = sem("wqkv_set")
        wf_high = sem("wf_high")
        wf_set = sem("wf_set")
        wo_set = sem("wo_set")
        bias_qk_set = sem("bias_qk_set")
        bias_o_set = sem("bias_o_set")
        bias_f_set = sem("bias_f_set")
        kvq_mm = sem("kvq_mm")
        expk_done = sem("expk_done")
        expq_done = sem("expq_done")
        reluq_done = sem("reluq_done")
        mink_done = sem("mink_done")
        minq_done = sem("minq_done")
        K_done = sem("K_done")
        KV_done = sem("KV_done")
        Q_done = sem("Q_done")
        sums_done = sem("sums_done")
        lnz_done = sem("lnz_done")
        rz_done = sem("rz_done")
        V_done = sem("V_done")
        wo_mm = sem("wo_mm")
        wf1_mm = sem("wf1_mm")
        hid_done = sem("hid_done")
        wf2_mm = sem("wf2_mm")
        gelu_done = [sem("gelu1_done"), sem("gelu2_done")]
        y_done = [sem("y1_done"), sem("y2_done")]
        yh_done = [sem("yh1_done"), sem("yh2_done")]
        yl_done = [sem("yl1_done"), sem("yl2_done")]
        centre_mm = [sem("centre1_mm"), sem("centre2_mm")]
        cs_done = [sem("cs1_done"), sem("cs2_done")]
        sq_done = [sem("sq1_done"), sem("sq2_done")]
        var_mm = [sem("var1_mm"), sem("var2_mm")]
        ve_done = [sem("ve1_done"), sem("ve2_done")]
        rs_done = [sem("rs1_done"), sem("rs2_done")]
        turn_mm = [sem("turn1_mm"), sem("turn2_mm")]
        rsh_done = [sem("rsh1_done"), sem("rsh2_done")]
        rsl_done = [sem("rsl1_done"), sem("rsl2_done")]
        spread_mm = [sem("spread1_mm"), sem("spread2_mm")]
        norm_done = [sem("norm1_done"), sem("norm2_done")]
        xf_done = [sem("x1_done"), sem("x2_done")]
        xh_done = [sem("x1h_done"), sem("xrh_done")]
        xl_done = [sem("x1l_done"), sem("xrl_done")]
        out_stored = sem("out_stored")
        moe_loaded = sem("moe_loaded")
        x0_loaded = sem("x0_loaded")
        prep = sem("prep")
        prep_mm = sem("prep_mm")
        prep_copied = sem("prep_copied")
        z_done = sem("z_done")
        zt_mm = sem("zt_mm")
        stats_done = [sem(f"stats{n}_done") for n in ("_z", "_mix", "_sum")]
        moments_step = [sem(f"moments{n}_step") for n in ("_z", "_mix", "_sum")]
        var_eps_done = [sem(f"var_eps{n}_done") for n in ("_z", "_mix", "_sum")]
        rstd_done = [sem(f"rstd{n}_done") for n in ("_z", "_mix", "_sum")]
        minus_mean_done = [sem(f"minus_mean{n}_done") for n in ("_z", "_mix", "_sum")]
        x_var_done = sem("x_var_done")
        x_rstd_done = sem("x_rstd_done")
        xt_done = sem("xt_done")
        xe_mm = sem("xe_mm")
        xe_h_done = sem("xe_h_done")
        xe_l_done = sem("xe_l_done")
        router_mm = sem("router_mm")
        gram_mm = sem("gram_mm")
        square_done = sem("square_done")
        hid_ln_done = sem("hid_ln_done")
        moe_eps_set = sem("moe_eps_set")
        hid_std_done = sem("hid_std_done")
        std_split = sem("std_split")
        std_turned = sem("std_turned")
        std_rows_done = sem("std_rows_done")
        gate_step = sem("gate_step")
        exps_done = sem("exps_done")
        expert_mm = sem("expert_mm")
        relu_done = sem("relu_done")
        expert_out_mm = sem("expert_out_mm")
        mix_done = sem("mix_done")
        mix_normed = sem("mix_normed")
        mix_scaled = sem("mix_scaled")
        xb_done = sem("xb_done")
        sum_done = sem("sum_done")
        result_done = sem("result_done")
        mhalf_set = sem("mhalf_set")
        pad_set = sem("pad_set")

        def upto(it, k, h):
            n = it * 8 + (2 * k + h + 1)
            return min(n, 2 * UNITS) if isinstance(n, int) else n

        def kvq_upto(it, k, h):
            return it * 8 + (2 * k + h + 9)

        SPLITS = 2 * UNITS + 2

        def splits(which, it, k):
            return which == 0 or kvq_upto(it, k, 0) < SPLITS if isinstance(it, int) else True

        def splits_upto(which, it, k, h):
            if which == 0:
                return upto(it, k, h)
            n = kvq_upto(it, k, h)
            return min(n, SPLITS) if isinstance(n, int) else n

        def units_upto(it, k):
            return it * 4 + (k + 1)

        def hid_upto(it, k, m):
            return it * 32 + (8 * k + m + 1)

        def after(engine, semaphore, n):
            if not isinstance(n, int) or n > 0:
                engine.wait_ge(semaphore, n)

        def layer(it, k):
            return it + k // 4

        def half(h):
            return slice(h * CH, (h + 1) * CH)

        def ring(k, h):
            c = 2 * (k % 2) + h
            return slice(c * CH, (c + 1) * CH)

        def chunk(k, h):
            c = 2 * (k % 4) + h
            return slice(c * CH, (c + 1) * CH)

        def param(l, j, table=par):
            return table[:, bass.ds(l * NPAR + j, 1)]

        ORDER = ((1, 0, 2), (1, 1, 2), (0, 0, 0), (0, 1, 0))

        def earlier(which, it, k, h, stride):
            at = [o[:2] for o in ORDER].index((which, h))
            place = 4 * (k + ORDER[at][2]) + at
            while True:
                place -= stride
                w, g, back = ORDER[place % 4]
                unit = place // 4 - back
                if not isinstance(it, int):
                    return w, upto(it, unit, g)
                if place + 16 * it < 0:
                    return w, 0
                if 0 <= 4 * it + unit < UNITS:
                    return w, upto(it, unit, g)

        def projected(it, k):
            return k - 2 if isinstance(it, int) and it == 0 and k < 2 else k - 3

        def run(engine, step):
            step(0, 0, True, False, False, True)
            step(0, 1, True, True, False, True)
            step(0, 2, True, True, True, False)
            with engine.Fori(0, LAYERS - 1) as it:
                for k in range(3, 7):
                    step(it, k, True, True, True, True)
            step(LAYERS - 1, 3, True, True, True, False)
            step(LAYERS - 1, 4, False, True, True, False)
            step(LAYERS - 1, 5, False, False, True, False)

        MIXED = (O[1], L[1])
        GATE_STEPS = 19
        MOMENT_STEPS = 6
        PREP_STEPS = 18

        def run_moe(engine, step):
            step(0, 0, True, True, False, False)
            step(0, 1, True, True, True, False)
            step(0, 2, True, True, True, True)
            with engine.Fori(0, 2) as it:
                step(it, 3, True, True, True, True)
                step(it, 4, True, True, True, True)
            step(2, 3, False, True, True, True)
            step(2, 4, False, False, True, True)
            step(2, 5, False, False, False, True)

        def upto_chunk(it, k):
            return it * 2 + (k + 1)

        def tile(t, at=0):
            return slice(at + t * P, at + (t + 1) * P)

        def par_tile(k, t):
            return tile(t, k % 2 * CH)

        def par_tiles(k):
            return slice(k % 2 * TILES, (k % 2 + 1) * TILES)

        def by_tile(ap):
            return ap.rearrange("p (t e) -> p t e", t=TILES)

        def over_experts(ap):
            return ap.unsqueeze(2).to_broadcast([P, TILES, EXPERTS])

        def over_tiles(ap, n):
            return ap.unsqueeze(1).to_broadcast([P, TILES, n])

        block = ctx.enter_context(nc.Block())

        @block.sync
        def _(sp):
            sp.dma_start(par[:, 0:LAYERS * NPAR], par_in).then_inc(par_loaded, 16)
            sp.dma_start(x[:, 0:CH], x_in[:, 0:CH]).then_inc(x_loaded[0], 16)
            sp.dma_start(wraw[:, 0:WCOLS], w_in[:, 0:WCOLS]).then_inc(wfirst_loaded, 16)
            for c in range(1, 8):
                cols = slice(c * CH, (c + 1) * CH)
                sp.dma_start(x[:, cols], x_in[:, cols]).then_inc(x_loaded[c], 16)
            for l in range(1, LAYERS):
                cols = slice(l * WCOLS, (l + 1) * WCOLS)
                sp.dma_start(wraw[:, cols], w_in[:, cols]).then_inc(wrest_loaded, 16)
            sp.wait_ge(wqkv_set, LAYERS)
            sp.wait_ge(wo_set, LAYERS)
            sp.wait_ge(wf_set, 2 * LAYERS)
            sp.dma_start(w1, w1_in).then_inc(moe_loaded, 16)
            sp.dma_start(w2, w2_in).then_inc(moe_loaded, 16)
            sp.dma_start(g_all, row_in[0:1, 0:EW].to_broadcast([P, EW])).then_inc(moe_loaded, 16)
            sp.dma_start(b_raw, row_in[0:1, EW:2 * EW].to_broadcast([3 * EXPERTS, EW])).then_inc(moe_loaded, 16)
            sp.dma_start(wraw[:, 7 * EW:7 * EW + 2 * P],
                         row_in[0:1, 2 * EW:].to_broadcast([P, 2 * P])).then_inc(moe_loaded, 16)
            sp.dma_start(moe_small[:, :], moe_in).then_inc(moe_loaded, 16)
            sp.wait_ge(V_done, 2 * UNITS)
            sp.dma_start(x0[:, :], x_in).then_inc(x0_loaded, 16)

            def step(it, k, enters, routes, mixes, ends):
                if ends:
                    c = bass.ds((it * 2 + (k - 2)) * TILES, TILES)
                    sp.wait_ge(result_done, upto_chunk(it, k - 2) * TILES)
                    sp.dma_start(out[:, c, :], result[:, par_tile(k, 0).start:par_tile(k, 0).start + CH]
                                 .rearrange("p (t d) -> p t d", t=TILES)).then_inc(out_stored, 16)

            run_moe(sp, step)
            sp.wait_ge(out_stored, 16 * CHUNKS)

        @block.scalar
        def _(act):
            act.dma_start(consts[:, :], const_in[:, 0:2 * P]).then_inc(par_loaded, 16)
            act.dma_start(masks[:, :], const_in[:, 2 * P + 2 * TILES * P:]).then_inc(par_loaded, 16)
            act.dma_start(hid[0:LOW + 2 * TILES, 0:2 * TILES * P], const_in[0:LOW + 2 * TILES, 2 * P:2 * P + 2 * TILES * P]).then_inc(par_loaded, 16)
            nc.scalar.preload_act_table_set("natural_log_exp_and_others")
            act.wait_ge(par_loaded, 64)
            act.wait_ge(consts_set, 6)

            def exp_kq(it, k, h):
                n = kvq_upto(it, k, h)
                act.wait_ge(bias_qk_set, layer(it, k) + 2)
                act.wait_ge(kvq_mm, 3 * n - 2)
                after(act, K_done, n - 2)
                nc.scalar.activation(expk[:, half(h)], K_BANK[h][:, :], ACT.Exp,
                                     bias=bias_qk[:, BK:BK + 1]).then_inc(expk_done, 1)
                act.wait_ge(kvq_mm, 3 * n - 1)
                after(act, Q_done, n - 2)
                nc.scalar.activation(expq[:, half(h)], Q_BANK[h][:, :], ACT.Exp,
                                     bias=bias_qk[:, BQ:BQ + 1]).then_inc(expq_done, 1)
                nc.scalar.activation(reluq[:, half(h)], Q_BANK[h][:, :], ACT.Relu,
                                     bias=bias_qk[:, BQ:BQ + 1]).then_inc(reluq_done, 1)

            def recip_z(it, k, h):
                n = upto(it, k, h)
                b = k % 4 // 2
                act.wait_ge(sums_done, it * 4 + 2 * (k // 2 + 1))
                act.wait_ge(Q_done, it * 8 + 2 * k + h + 1)
                after(act, V_done, n - 2)
                nc.scalar.activation(rz[:, half(h)], Q[:, chunk(k, h)], ACT.Ln, bias=epsz[:, :],
                                     scale=ks[:, b:b + 1]).then_inc(lnz_done, 1)
                act.wait_ge(lnz_done, n)
                nc.scalar.activation(rz[:, half(h)], rz[:, half(h)], ACT.Exp,
                                     scale=-1.0).then_inc(rz_done, 1)

            def centred(which, it, k, h):
                n = upto(it, k, h)
                act.wait_ge(centre_mm[which], n)
                after(act, xf_done[which], n - 2)
                after(act, xh_done[which], splits_upto(which, it, k - 1, h))
                nc.scalar.activation(cs[which][:, half(h)], C[:, :], ACT.Copy).then_inc(cs_done[which], 1)
                w, m = earlier(which, it, k, h, 2)
                after(act, var_mm[w], m)
                nc.scalar.activation(sq[:, half(h)], C[:, :], ACT.Square).then_inc(sq_done[which], 1)

            def gelu_attend(it, k, h):
                n = upto(it, k, h)
                act.wait_ge(bias_o_set, layer(it, k) + 1)
                act.wait_ge(wo_mm, n)
                after(act, yl_done[0], n - 2)
                nc.scalar.activation(y[0][:, half(h)], O[h][:, :], GELU,
                                     bias=bias_o[:, :]).then_inc(gelu_done[0], 1)

            def gelu_hidden(it, k, m):
                act.wait_ge(bias_f_set, layer(it, k) + 1)
                act.wait_ge(wf1_mm, hid_upto(it, k, m))
                after(act, wf2_mm, upto(it, k - 1, m // FB))
                nc.scalar.activation(hid[:, m * CH:(m + 1) * CH], HIDDEN[m % 3][:, :], GELU,
                                     bias=bias_f[:, 1 + m % FB:2 + m % FB]).then_inc(hid_done, 1)

            def gelu_feed(it, k, h):
                n = upto(it, k, h)
                act.wait_ge(wf2_mm, n)
                after(act, yl_done[1], n - 2)
                nc.scalar.activation(y[1][:, half(h)], O[h][:, :], GELU,
                                     bias=bias_f[:, 0:1]).then_inc(gelu_done[1], 1)

            def prepare():
                for n in range(2):
                    act.wait_ge(prep_mm, 1 + n)
                    nc.scalar.activation(w1ct[:, n * CH:(n + 1) * CH], R[n][:, :], ACT.Copy,
                                         scale=H ** -0.5).then_inc(prep_copied, 1)

            def rows_of_std(it, k):
                n = upto_chunk(it, k)
                act.wait_ge(std_turned, n)
                after(act, expert_mm, (n - 1) * HB)
                nc.scalar.activation(std_rows, L[0][0:3 * EXPERTS, :], ACT.Copy).then_inc(std_rows_done, 1)

            def normalised(it, k):
                n = upto_chunk(it, k)
                act.wait_ge(rstd_done[0], n)
                act.wait_ge(minus_mean_done[0], n)
                act.wait_ge(zt_mm, n)
                if isinstance(n, int) and n <= 2:
                    act.wait_ge(y_done[1], 2 * UNITS)
                after(act, xb_done, n - 2)
                after(act, square_done, (n - 2) * TE)
                for t in range(TILES):
                    nc.scalar.activation(xt[:, par_tile(k, t)], C[:, tile(t)], ACT.Identity,
                                         bias=minus_mean[0][:, t:t + 1],
                                         scale=rstd[0][:, t:t + 1]).then_inc(xt_done, 1)

            def high_x(it, k):
                n = upto_chunk(it, k)
                act.wait_ge(xe_mm, n)
                after(act, expert_mm, (n - 2) * HB)
                nc.scalar.activation(xe_h[:, half(k % 2)], C[:, :], ACT.Copy).then_inc(xe_h_done, 1)

            def relu(it, k, m):
                n = upto_chunk(it, k)
                act.wait_ge(expert_mm, (n - 1) * HB + m + 1)
                after(act, expert_out_mm, (n - 1) * TILES)
                nc.scalar.activation(hid[:, m * CH:(m + 1) * CH], R[m % 3][:, :],
                                     ACT.Relu).then_inc(relu_done, 1)

            def norm_mix(it, k):
                n = upto_chunk(it, k)
                act.wait_ge(rstd_done[1], n)
                act.wait_ge(minus_mean_done[1], n)
                for t in range(TILES):
                    o = mix[:, par_tile(k, t)]
                    nc.scalar.activation(o, o, ACT.Identity, bias=minus_mean[1][:, t:t + 1],
                                         scale=rstd[1][:, t:t + 1]).then_inc(mix_normed, 1)

            def norm_sum(it, k):
                n = upto_chunk(it, k)
                act.wait_ge(rstd_done[2], n)
                act.wait_ge(minus_mean_done[2], n)
                after(act, out_stored, 16 * (n - 1))
                for t in range(TILES):
                    nc.scalar.activation(result[:, par_tile(k, t)], mix[:, par_tile(k, t)], ACT.Identity,
                                         bias=minus_mean[2][:, t:t + 1],
                                         scale=rstd[2][:, t:t + 1]).then_inc(result_done, 1)

            def roots_of_hidden(it, k):
                n = upto_chunk(it, k)
                act.wait_ge(square_done, n * TE)
                act.wait_ge(moe_eps_set, 1)
                nc.scalar.activation(hid_var[:, :], hid_var[:, :], ACT.Ln, bias=moe_eps[:, :]).then_inc(hid_ln_done, 1)
                act.wait_ge(hid_ln_done, n)
                after(act, std_split, 3 * (n - 1))
                nc.scalar.activation(hid_std[:, 0:TE], hid_var[:, :], ACT.Exp, scale=0.5).then_inc(hid_std_done, 1)
                after(act, gate_step, (n - 1) * GATE_STEPS)
                nc.scalar.activation(hid_std[:, TE:2 * TE], hid_var[:, :], ACT.Exp, scale=-0.5).then_inc(hid_std_done, 1)

            def exp_logits(it, k):
                n = upto_chunk(it, k)
                act.wait_ge(gate_step, (n - 1) * GATE_STEPS + 4)
                nc.scalar.activation(exps[:, :], logits[:, :], ACT.Exp).then_inc(exps_done, 1)

            def step(it, k, attends, feeds, ends, projects):
                nc.scalar.preload_act_table_set("natural_log_exp_and_others")
                if projects:
                    exp_kq(it, projected(it, k), 0)
                    exp_kq(it, projected(it, k), 1)
                if ends:
                    centred(1, it, k - 2, 0)
                    centred(1, it, k - 2, 1)
                if k == 5 and not projects:
                    normalised(0, 0)
                    high_x(0, 0)
                if attends:
                    recip_z(it, k, 0)
                    recip_z(it, k, 1)
                if attends or feeds:
                    nc.scalar.preload_act_table_set("gelu_apprx_tanh_and_others")
                if feeds:
                    gelu_hidden(it, k - 1, 0)
                if attends:
                    gelu_attend(it, k, 0)
                if feeds:
                    gelu_hidden(it, k - 1, 1)
                    gelu_hidden(it, k - 1, 2)
                    gelu_hidden(it, k - 1, 3)
                if attends:
                    gelu_attend(it, k, 1)
                    centred(0, it, k, 0)
                if feeds:
                    gelu_hidden(it, k - 1, 4)
                if attends:
                    centred(0, it, k, 1)
                if feeds:
                    gelu_hidden(it, k - 1, 5)
                    gelu_feed(it, k - 1, 0)
                    gelu_hidden(it, k - 1, 6)
                    gelu_hidden(it, k - 1, 7)
                    gelu_feed(it, k - 1, 1)
                if k == 4 and not projects:
                    prepare()

            for c in range(4):
                exp_kq(0, c // 2 - 4, c % 2)
            run(nc.scalar, step)


            def step(it, k, enters, routes, mixes, ends):
                for m in range(HB):
                    if mixes:
                        relu(it, k - 1, m)
                    if ends and m == 4:
                        norm_mix(it, k - 2)
                    if enters and m == 6:
                        normalised(it, k + 1)
                if routes:
                    roots_of_hidden(it, k)
                    exp_logits(it, k)
                if enters:
                    high_x(it, k + 1)
                if routes:
                    rows_of_std(it, k)
                if ends:
                    norm_sum(it, k - 2)

            run_moe(nc.scalar, step)

        @block.tensor
        def _(pe):
            pe.wait_ge(par_loaded, 64)
            pe.wait_ge(consts_set, 6)

            def product(bank, w_h, w_l, a_h, a_l):
                nc.tensor.matmul(bank, w_h, a_h, start=True, stop=False)
                nc.tensor.matmul(bank, w_h, a_l, start=False, stop=False)
                return nc.tensor.matmul(bank, w_l, a_h, start=False, stop=True)

            def kvq(it, k, h):
                n = kvq_upto(it, k, h)
                pe.wait_ge(xh_done[1], n)
                pe.wait_ge(xl_done[1], n)
                pe.wait_ge(wqkv_set, layer(it, k) + 2)
                first_layer = isinstance(it, int) and 4 * it + k < 0
                for j, bank, used, m in ((1, K_BANK[h], K_done, 6), (0, Q_BANK[h], reluq_done, 7),
                                         (2, V_BANK, KV_done, 5)):
                    if bank is V_BANK and (h == 1 or first_layer):
                        after(pe, used, n - 1)
                    elif first_layer:
                        after(pe, used, n - 2)
                        if k == -1 and h == 1:
                            pe.wait_ge(gelu_done[0], 2)
                    elif h == 0:
                        pe.wait_ge(hid_done, hid_upto(it, k + 1, m))
                    else:
                        pe.wait_ge(gelu_done[1], upto(it, k + 1, 1 if j == 0 else 0))
                    w = slice(j * P, (j + 1) * P)
                    product(bank[:, :], wqkv_h[:, w], wqkv_l[:, w], xr_h[:, ring(k, h)],
                            xr_l[:, ring(k, h)]).then_inc(kvq_mm, 1)

            def attend_out(it, k, h, projects):
                n = upto(it, k, h)
                pe.wait_ge(V_done, n)
                pe.wait_ge(wo_set, layer(it, k) + 1)
                after(pe, gelu_done[1], n - 4)
                if projects:
                    pe.wait_ge((K_done, reluq_done)[h], kvq_upto(it, projected(it, k), 1))
                nc.tensor.matmul(O[h][:, :], wo[:, :], V[:, half(h)], start=True,
                                 stop=True).then_inc(wo_mm, 1)

            def hidden(it, k, m):
                h, j = m // FB, m % FB
                pe.wait_ge(xh_done[0], upto(it, k, h))
                pe.wait_ge(xl_done[0], upto(it, k, h))
                pe.wait_ge(wf_set, 2 * (layer(it, k) + 1))
                if m >= 3:
                    pe.wait_ge(hid_done, hid_upto(it, k, m - 3))
                elif isinstance(it, int) and 4 * it + k > 0:
                    pe.wait_ge(hid_done, hid_upto(it, k - 1, (6, 7, 5)[m]))
                else:
                    n = 8 if isinstance(it, int) else kvq_upto(it, k - 2, 1)
                    pe.wait_ge((K_done, reluq_done, KV_done)[m], n - (1, 1, 0)[m])
                w = slice(j * P, (j + 1) * P)
                product(HIDDEN[m % 3][:, :], wf1_h[:, w], wf1_l[:, w], x1_h[:, ring(k, h)],
                        x1_l[:, ring(k, h)]).then_inc(wf1_mm, 1)

            def feed_out(it, k, m):
                h, j = m // FB, m % FB
                if j == 0:
                    pe.wait_ge(gelu_done[0], upto(it, k + 1, h))
                pe.wait_ge(hid_done, hid_upto(it, k, m))
                mm = nc.tensor.matmul(O[h][:, :], wf2[:, j * P:(j + 1) * P], hid[:, m * CH:(m + 1) * CH],
                                      start=(j == 0), stop=(j == FB - 1))
                if j == FB - 1:
                    mm.then_inc(wf2_mm, 1)

            def centre(which, it, k, h):
                n = upto(it, k, h)
                pe.wait_ge(yh_done[which], n)
                pe.wait_ge(yl_done[which], n)
                w, m = earlier(which, it, k, h, 1)
                after(pe, sq_done[w], m)
                nc.tensor.matmul(C[:, :], cen[:, :], y_h[:, half(h)], start=True, stop=False)
                nc.tensor.matmul(C[:, :], cen[:, :], y_l[:, half(h)], start=False,
                                 stop=True).then_inc(centre_mm[which], 1)

            def variance(which, it, k):
                w, m = earlier(which, it, k, 0, 2)
                after(pe, norm_done[w], m)
                for h in range(2):
                    pe.wait_ge(sq_done[which], upto(it, k, h))
                    for t in range(TILES):
                        c = h * TILES + t
                        mm = nc.tensor.matmul(L[0][:, c:c + 1], sq[:, c * P:(c + 1) * P], mean1[:, :],
                                              start=True, stop=True)
                    mm.then_inc(var_mm[which], 1)

            def turn(which, it, k):
                pe.wait_ge(rs_done[which], units_upto(it, k))
                nc.tensor.transpose(L[0][0:2 * TILES, P:2 * P], rs[which][:, :],
                                    ident).then_inc(turn_mm[which], 1)

            def spread(which, it, k):
                pe.wait_ge(rsh_done[which], units_upto(it, k))
                pe.wait_ge(rsl_done[which], units_upto(it, k))
                for h in range(2):
                    w, m = earlier(which, it, k, h, 2)
                    after(pe, norm_done[w], m)
                    for t in range(TILES):
                        tile = slice(t * P, (t + 1) * P)
                        pick = sel[:, (h * TILES + t) * P:(h * TILES + t + 1) * P]
                        mm = nc.tensor.matmul(L[h][:, tile], pick, rs_hl[:, :], start=True, stop=True)
                    mm.then_inc(spread_mm[which], 1)

            def prepare():
                pe.wait_ge(moe_loaded, 16 * 6)
                pe.wait_ge(prep, 6)
                pe.wait_ge(hid_done, FB * 2 * UNITS)
                for m in range(HB):
                    mm = nc.tensor.transpose(R[m // 4][:, tile(m % 4)], w1c[:, tile(m)], ident)
                    if m % 4 == 3:
                        mm.then_inc(prep_mm, 1)
                pe.wait_ge(prep_copied, 2)
                for m in range(HB):
                    mm = nc.tensor.matmul(R[2][:, tile(m // 2)], w1ct[:, tile(m)], w1ct[:, tile(m)],
                                          start=(m % 2 == 0), stop=(m % 2 == 1))
                mm.then_inc(prep_mm, 1)
                nc.tensor.matmul(R[0][:, 0:EXPERTS], rn_b_all[:, :], moe_small[:, 2:2 + EXPERTS], start=True,
                                 stop=True).then_inc(prep_mm, 1)

            def turn_std(it, k):
                n = upto_chunk(it, k)
                pe.wait_ge(std_split, 3 * n)
                if isinstance(n, int) and n == 1:
                    pe.wait_ge(norm_done[1], 2 * UNITS)
                else:
                    pe.wait_ge(std_rows_done, n - 1)
                for t in range(TILES):
                    mm = nc.tensor.transpose(L[0][0:3 * EXPERTS, tile(t)],
                                             std_parts[:, 3 * EXPERTS * t:3 * EXPERTS * (t + 1)], ident)
                mm.then_inc(std_turned, 1)

            def turn_z(it, k):
                n = upto_chunk(it, k)
                pe.wait_ge(z_done, n)
                if isinstance(n, int) and n == 1:
                    pe.wait_ge(sq_done[0], 2 * UNITS)
                    pe.wait_ge(sq_done[1], 2 * UNITS)
                else:
                    pe.wait_ge(xe_l_done, n - 1)
                for t in range(TILES):
                    mm = nc.tensor.transpose(C[:, tile(t)], z[:, par_tile(k, t)], ident)
                mm.then_inc(zt_mm, 1)

            def turn_x(it, k):
                n = upto_chunk(it, k)
                pe.wait_ge(xt_done, n * TILES)
                for t in range(TILES):
                    mm = nc.tensor.transpose(C[:, tile(t)], xt[:, par_tile(k, t)], ident)
                mm.then_inc(xe_mm, 1)

            def expert_hidden(it, k, m):
                n = upto_chunk(it, k)
                last = (n - 1) * HB
                if m >= 3:
                    pe.wait_ge(relu_done, last + m - 2)
                else:
                    after(pe, relu_done, last + (-1, 0, -2)[m])
                w = tile(m)
                c = half(k % 2)
                nc.tensor.matmul(R[m % 3][:, :], w1_h[:, w], xe_h[:, c], start=True, stop=False)
                nc.tensor.matmul(R[m % 3][:, :], w1_h[:, w], xe_l[:, c], start=False, stop=False)
                nc.tensor.matmul(R[m % 3][:, :], w1_l[:, w], xe_h[:, c], start=False, stop=False)
                pe.wait_ge(std_rows_done, n)
                nc.tensor.matmul(R[m % 3][:, :], b_rows[:, w], std_rows, start=False,
                                 stop=True).then_inc(expert_mm, 1)

            def route(it, k):
                n = upto_chunk(it, k)
                pe.wait_ge(xe_l_done, n)
                pe.wait_ge(square_done, n * TE)
                for t in range(TILES):
                    o = O[0][:, t * EXPERTS:(t + 1) * EXPERTS]
                    nc.tensor.matmul(o, xe_h[:, par_tile(k, t)], rw_h[:, :], start=True, stop=False)
                    nc.tensor.matmul(o, xe_l[:, par_tile(k, t)], rw_h[:, :], start=False, stop=False)
                    mm = nc.tensor.matmul(o, xe_h[:, par_tile(k, t)], rw_l[:, :], start=False, stop=True)
                mm.then_inc(router_mm, 1)

            def gram(it, k, t):
                n = upto_chunk(it, k)
                pe.wait_ge(xe_l_done, n)
                if t == 0:
                    after(pe, gate_step, (n - 2) * GATE_STEPS + 1)
                else:
                    pe.wait_ge(square_done, (n - 1) * TE + t * EXPERTS)
                nc.tensor.matmul(O[0][:, :], xe_h[:, par_tile(k, t)], gram_h, start=True, stop=False)
                nc.tensor.matmul(O[0][:, :], xe_l[:, par_tile(k, t)], gram_h, start=False, stop=False)
                nc.tensor.matmul(O[0][:, :], xe_h[:, par_tile(k, t)], gram_l, start=False,
                                 stop=True).then_inc(gram_mm, 1)

            def expert_out(it, k, t):
                n = upto_chunk(it, k)
                pe.wait_ge(relu_done, n * HB)
                after(pe, mix_done, ((n - 1) * TILES + t - 1) * EXPERTS)
                for m in range(HB):
                    mm = nc.tensor.matmul(MIXED[t % 2][:, tile(m // 2)], hid[:, tile(t, m * CH)], w2[:, tile(m)],
                                          start=(m % 2 == 0), stop=(m % 2 == 1))
                mm.then_inc(expert_out_mm, 1)

            def step(it, k, attends, feeds, ends, projects):
                if projects:
                    kvq(it, projected(it, k), 0)
                if feeds:
                    spread(0, it, k - 1)
                if ends:
                    centre(1, it, k - 2, 0)
                if projects:
                    kvq(it, projected(it, k), 1)
                if ends:
                    centre(1, it, k - 2, 1)
                if feeds:
                    hidden(it, k - 1, 0)
                    hidden(it, k - 1, 1)
                if ends:
                    variance(1, it, k - 2)
                if k == 5 and not projects:
                    turn_z(0, 0)
                if feeds:
                    hidden(it, k - 1, 2)
                if attends:
                    attend_out(it, k, 0, projects)
                    attend_out(it, k, 1, projects)
                if feeds:
                    hidden(it, k - 1, 3)
                    feed_out(it, k - 1, 0)
                    hidden(it, k - 1, 4)
                    hidden(it, k - 1, 5)
                    feed_out(it, k - 1, 1)
                if ends:
                    turn(1, it, k - 2)
                if attends:
                    centre(0, it, k, 0)
                if feeds:
                    feed_out(it, k - 1, 2)
                    feed_out(it, k - 1, 3)
                if attends:
                    centre(0, it, k, 1)
                if ends:
                    spread(1, it, k - 2)
                if k == 5 and not projects:
                    turn_x(0, 0)
                if feeds:
                    feed_out(it, k - 1, 4)
                    hidden(it, k - 1, 6)
                    hidden(it, k - 1, 7)
                if attends:
                    variance(0, it, k)
                if feeds:
                    feed_out(it, k - 1, 5)
                    feed_out(it, k - 1, 6)
                    feed_out(it, k - 1, 7)
                if attends:
                    turn(0, it, k)
                if k == 4 and not projects:
                    prepare()

            for c in range(4):
                kvq(0, c // 2 - 4, c % 2)
            run(nc.tensor, step)


            pe.wait_ge(prep, PREP_STEPS)

            def step(it, k, enters, routes, mixes, ends):
                for m in range(HB):
                    if mixes:
                        expert_hidden(it, k - 1, m)
                    if routes and m % 2 == 0:
                        gram(it, k, m // 2)
                    if enters and m == 1:
                        turn_z(it, k + 1)
                if routes:
                    route(it, k)
                if enters:
                    turn_x(it, k + 1)
                if mixes:
                    expert_out(it, k - 1, 0)
                if routes:
                    turn_std(it, k)
                if mixes:
                    expert_out(it, k - 1, 1)
                    expert_out(it, k - 1, 2)
                    expert_out(it, k - 1, 3)

            run_moe(nc.tensor, step)

        @block.vector
        def _(dve):
            nc.vector.memset(mean1[:, :], 1.0 / P).then_inc(consts_set, 1)
            nc.vector.memset(epsz[:, :], EPS_Z).then_inc(consts_set, 1)
            nc.vector.memset(rs_hl[:, :].bitcast(F32), 0.0).then_inc(consts_set, 1)
            dve.wait_ge(par_loaded, 64)
            nc.vector.tensor_copy(cen[:, :], consts[:, P:2 * P]).then_inc(consts_set, 1)
            nc.vector.tensor_copy(sel[:, :], hid[0:LOW + 2 * TILES, 0:2 * TILES * P]).then_inc(consts_set, 1)
            nc.vector.tensor_scalar(bias1[:, :], par[:, 0:LAYERS * NPAR], 1.0, None, ALU.add).then_inc(consts_set, 1)
            dve.wait_ge(consts_set, 6)

            def install_qkv(l, it, k):
                raw = wraw[:, bass.ds(l * WCOLS, QKV)]
                dve.wait_ge(kvq_mm, 3 * kvq_upto(it, k, 1))
                nc.vector.tensor_copy(wqkv_h[:, :], raw).then_inc(wqkv_high, 1)
                dve.wait_ge(wqkv_high, l + 1)
                nc.vector.tensor_tensor(wqkv_l[:, :], raw, wqkv_h[:, :].bitcast(F32),
                                        ALU.subtract).then_inc(wqkv_set, 1)

            def install_wo(l, it, k):
                after(dve, wo_mm, upto(it, k, 1))
                nc.vector.tensor_copy(wo[:, :], wraw[:, bass.ds(l * WCOLS + WO, P)]).then_inc(wo_set, 1)

            def install_wf(l, it, k):
                raw = wraw[:, bass.ds(l * WCOLS + WF1, FB * P)]
                after(dve, wf1_mm, hid_upto(it, k, 7))
                nc.vector.tensor_copy(wf1_h[:, :], raw).then_inc(wf_high, 1)
                after(dve, wf2_mm, upto(it, k, 1))
                nc.vector.tensor_copy(wf2[:, :], wraw[:, bass.ds(l * WCOLS + WF2, FB * P)]).then_inc(wf_set, 1)
                dve.wait_ge(wf_high, l + 1)
                nc.vector.tensor_tensor(wf1_l[:, :], raw, wf1_h[:, :].bitcast(F32),
                                        ALU.subtract).then_inc(wf_set, 1)

            def install_bias_qk(l):
                nc.vector.tensor_copy(bias_qk[:, :], par[:, bass.ds(l * NPAR + BQ, 2)]).then_inc(bias_qk_set, 1)

            def install_bias_o(l):
                nc.vector.tensor_copy(bias_o[:, :], par[:, bass.ds(l * NPAR + BO, 1)]).then_inc(bias_o_set, 1)

            def install_bias_f(l):
                nc.vector.tensor_copy(bias_f[:, :], par[:, bass.ds(l * NPAR + BF2, 1 + FB)]).then_inc(bias_f_set, 1)

            def kvq_sums(it, k, h):
                n = kvq_upto(it, k, h)
                l = layer(it, k) + 1
                c = 2 * (k % 4) + h
                dve.wait_ge(expk_done, n)
                nc.vector.tensor_scalar(expk[:, half(h)], expk[:, half(h)], 1.0, None,
                                        ALU.min).then_inc(mink_done, 1)
                dve.wait_ge(mink_done, n)
                nc.vector.scalar_tensor_tensor(out=Kt[:, half(h)], in0=K_BANK[h][:, :], scalar=param(l, BK, bias1),
                                               in1=expk[:, half(h)], op0=ALU.add, op1=ALU.max,
                                               accum_out=ksp[:, c:c + 1]).then_inc(K_done, 1)
                dve.wait_ge(kvq_mm, 3 * n)
                dve.wait_ge(K_done, n)
                nc.vector.scalar_tensor_tensor(out=Kt[:, half(h)], in0=V_BANK[:, :], scalar=param(l, BV),
                                               in1=Kt[:, half(h)], op0=ALU.add, op1=ALU.mult,
                                               accum_out=kvp[:, c:c + 1]).then_inc(KV_done, 1)
                if k % 2 == 1 and h == 1:
                    b = k % 4 // 2
                    dve.wait_ge(KV_done, n)
                    nc.vector.tensor_reduce(ks[:, b:b + 1], ksp[:, 4 * b:4 * b + 4], AX.X,
                                            ALU.add).then_inc(sums_done, 1)
                    nc.vector.tensor_reduce(kv[:, b:b + 1], kvp[:, 4 * b:4 * b + 4], AX.X,
                                            ALU.add).then_inc(sums_done, 1)

            def kvq_q(it, k, h):
                n = kvq_upto(it, k, h)
                dve.wait_ge(expq_done, n)
                nc.vector.tensor_scalar(expq[:, half(h)], expq[:, half(h)], 1.0, 1.0, ALU.min,
                                        ALU.subtract).then_inc(minq_done, 1)
                dve.wait_ge(minq_done, n)
                dve.wait_ge(reluq_done, n)
                nc.vector.scalar_tensor_tensor(out=Q[:, chunk(k, h)], in0=expq[:, half(h)], scalar=1.0,
                                               in1=reluq[:, half(h)], op0=ALU.add,
                                               op1=ALU.add).then_inc(Q_done, 1)

            def attend(it, k, h):
                n = upto(it, k, h)
                b = k % 4 // 2
                dve.wait_ge(rz_done, n)
                dve.wait_ge(sums_done, it * 4 + 2 * (k // 2 + 1))
                after(dve, wo_mm, n - 2)
                nc.vector.scalar_tensor_tensor(out=V[:, half(h)], in0=Q[:, chunk(k, h)], scalar=kv[:, b:b + 1],
                                               in1=rz[:, half(h)], op0=ALU.mult,
                                               op1=ALU.mult).then_inc(V_done, 1)

            def split_y(which, it, k, h):
                n = upto(it, k, h)
                dve.wait_ge(y_done[which], n)
                w, m = earlier(which, it, k, h, 2)
                after(dve, centre_mm[w], m)
                nc.vector.tensor_copy(y_h[:, half(h)], y[which][:, half(h)]).then_inc(yh_done[which], 1)
                dve.wait_ge(yh_done[which], n)
                nc.vector.tensor_tensor(y_l[:, half(h)], y[which][:, half(h)], y_h[:, half(h)].bitcast(F32),
                                        ALU.subtract).then_inc(yl_done[which], 1)

            def add_eps(which, it, k):
                dve.wait_ge(var_mm[which], upto(it, k, 1))
                nc.vector.tensor_scalar(ve[which][:, :], L[0][:, 0:2 * TILES], EPS_LN, None,
                                        ALU.add).then_inc(ve_done[which], 1)

            def split_rs(which, it, k):
                n = units_upto(it, k)
                turned = L[0][0:2 * TILES, P:2 * P]
                dve.wait_ge(turn_mm[which], n)
                w, m = earlier(which, it, k, 1, 2)
                after(dve, spread_mm[w], m)
                nc.vector.tensor_copy(rs_hl[0:2 * TILES, :], turned).then_inc(rsh_done[which], 1)
                dve.wait_ge(rsh_done[which], n)
                nc.vector.tensor_tensor(rs_hl[LOW:, :], turned, rs_hl[0:2 * TILES, :].bitcast(F32),
                                        ALU.subtract).then_inc(rsl_done[which], 1)

            def finish(which, it, k, h):
                n = upto(it, k, h)
                l = layer(it, k)
                s, b = ((S1, B1), (S2, B2))[which]
                full, high = ((x1[:, ring(k, h)], x1_h[:, ring(k, h)]),
                              (x[:, chunk(k, h)], xr_h[:, ring(k, h)]))[which]
                c = cs[which][:, half(h)]
                dve.wait_ge(spread_mm[which], n)
                dve.wait_ge(cs_done[which], n)
                nc.vector.scalar_tensor_tensor(out=c, in0=c, scalar=param(l, s), in1=L[h][:, :],
                                               op0=ALU.mult, op1=ALU.mult).then_inc(norm_done[which], 1)
                dve.wait_ge(norm_done[which], n)
                nc.vector.tensor_scalar(full, c, param(l, b), None, ALU.add).then_inc(xf_done[which], 1)
                if splits(which, it, k):
                    nc.vector.tensor_scalar(high, c, param(l, b), None, ALU.add).then_inc(xh_done[which], 1)

            EH = "p (e h) -> p e h"

            def prepare_w1():
                dve.wait_ge(moe_loaded, 16 * 6)
                nc.vector.tensor_copy(rn_b_all[:, :], moe_small[:, 1:2].to_broadcast([P, P])).then_inc(prep, 1)
                nc.vector.tensor_reduce(w1_mean[:, :], w1.rearrange(EH, e=EXPERTS), AX.X, ALU.add).then_inc(prep, 1)
                nc.vector.tensor_scalar(rw[:, :], moe_small[:, 2:2 + EXPERTS], moe_small[:, 0:1], None,
                                        ALU.mult).then_inc(prep, 1)
                dve.wait_ge(prep, 3)
                nc.vector.tensor_scalar(w1_mean[:, :], w1_mean[:, :], 1.0 / H, None, ALU.mult).then_inc(prep, 1)
                nc.vector.tensor_copy(rw_h[:, :], rw[:, :]).then_inc(prep, 1)
                dve.wait_ge(prep, 5)
                nc.vector.tensor_tensor(w1c.rearrange(EH, e=EXPERTS), w1.rearrange(EH, e=EXPERTS),
                                        w1_mean[:, :].unsqueeze(2).to_broadcast([P, EXPERTS, H]),
                                        ALU.subtract).then_inc(prep, 1)
                nc.vector.tensor_tensor(rw_l[:, :], rw[:, :], rw_h[:, :].bitcast(F32), ALU.subtract).then_inc(prep, 1)
                dve.wait_ge(prep, 7)
                nc.vector.tensor_tensor(w1, w1c, g_all, ALU.mult).then_inc(prep, 1)
                dve.wait_ge(kvq_mm, 3 * (2 * UNITS))
                dve.wait_ge(xl_done[1], SPLITS)
                dve.wait_ge(prep, 8)
                nc.vector.tensor_copy(w1_h, w1).then_inc(prep, 1)
                dve.wait_ge(prep, 9)
                nc.vector.tensor_tensor(w1_l, w1, w1_h.bitcast(F32), ALU.subtract).then_inc(prep, 1)

            def prepare_bias():
                dve.wait_ge(wf1_mm, FB * 2 * UNITS)
                nc.vector.tensor_copy(b_h, b_raw).then_inc(prep, 1)
                dve.wait_ge(prep, 11)
                mask_h = masks[0:3 * EXPERTS, 2 * TE:2 * TE + EXPERTS].unsqueeze(2).to_broadcast([3 * EXPERTS, EXPERTS, H])
                mask_l = masks[0:3 * EXPERTS, 2 * TE + EXPERTS:2 * TE + 2 * EXPERTS].unsqueeze(2).to_broadcast(
                    [3 * EXPERTS, EXPERTS, H])
                nc.vector.tensor_tensor(b_raw, b_raw, b_h.bitcast(F32), ALU.subtract).then_inc(prep, 1)
                nc.vector.tensor_tensor(b_part.rearrange(EH, e=EXPERTS), b_h.bitcast(F32).rearrange(EH, e=EXPERTS), mask_h,
                                        ALU.mult).then_inc(prep, 1)
                dve.wait_ge(prep, 13)
                nc.vector.tensor_tensor(b_raw.rearrange(EH, e=EXPERTS), b_raw.rearrange(EH, e=EXPERTS), mask_l,
                                        ALU.mult).then_inc(prep, 1)
                dve.wait_ge(prep, 14)
                nc.vector.tensor_tensor(b_rows, b_part, b_raw, ALU.add).then_inc(prep, 1)

            def prepare_gram():
                dve.wait_ge(prep_mm, 4)
                nc.vector.tensor_copy(router_b[:, :], R[0][:, 0:EXPERTS]).then_inc(prep, 1)
                dve.wait_ge(prep_mm, 4)
                nc.vector.tensor_copy(gram_h, R[2][:, :]).then_inc(prep, 1)
                dve.wait_ge(prep, 17)
                nc.vector.tensor_tensor(gram_l, R[2][:, :], gram_h.bitcast(F32), ALU.subtract).then_inc(prep, 1)

            Z, MIX, SUM = range(3)

            def statistics(which, it, k, source):
                n = upto_chunk(it, k)
                for t in range(TILES):
                    nc.vector.bn_stats(stats[which][:, 6 * t:6 * (t + 1)],
                                       source[:, tile(t)]).then_inc(stats_done[which], 1)
                    yield
                st = stats[which].rearrange("p (t s) -> p t s", s=6)
                step_done = moments_step[which]
                dve.wait_ge(stats_done[which], n * TILES)
                nc.vector.tensor_tensor(mean[which], st[:, :, 1], st[:, :, 4], ALU.add).then_inc(step_done, 1)
                nc.vector.tensor_tensor(apart[which], st[:, :, 1], st[:, :, 4], ALU.subtract).then_inc(step_done, 1)
                nc.vector.tensor_tensor(var[which], st[:, :, 2], st[:, :, 5], ALU.add).then_inc(step_done, 1)
                yield
                dve.wait_ge(step_done, (n - 1) * MOMENT_STEPS + 3)
                nc.vector.tensor_scalar(mean[which], mean[which], 0.5, None, ALU.mult).then_inc(step_done, 1)
                nc.vector.scalar_tensor_tensor(out=apart[which], in0=apart[which], scalar=0.25, in1=apart[which],
                                               op0=ALU.mult, op1=ALU.mult).then_inc(step_done, 1)
                yield
                dve.wait_ge(step_done, (n - 1) * MOMENT_STEPS + 5)
                nc.vector.scalar_tensor_tensor(out=var[which], in0=var[which], scalar=1.0 / P, in1=apart[which],
                                               op0=ALU.mult, op1=ALU.add).then_inc(step_done, 1)
                yield
                dve.wait_ge(step_done, n * MOMENT_STEPS)
                nc.vector.tensor_scalar(var_eps[which], var[which], EPS_OUT, None,
                                        ALU.add).then_inc(var_eps_done[which], 1)

            def add_input(it, k):
                n = upto_chunk(it, k)
                c = bass.ds((it * 2 + k) * CH, CH)
                dve.wait_ge(xf_done[1], 2 * UNITS - (7 if isinstance(n, int) and n == 1 else 0))
                if isinstance(n, int) and n == 1:
                    dve.wait_ge(yl_done[0], 2 * UNITS)
                else:
                    after(dve, zt_mm, n - 2)
                dve.wait_ge(x0_loaded, 16)
                nc.vector.tensor_tensor(z[:, half(k % 2)], x[:, c], x0[:, c], ALU.add).then_inc(z_done, 1)

            def stats_z(it, k):
                dve.wait_ge(zt_mm, upto_chunk(it, k))
                yield from statistics(Z, it, k, C)

            def scale_x(it, k):
                n = upto_chunk(it, k)
                dve.wait_ge(rstd_done[Z], n)
                dve.wait_ge(moments_step[Z], n * MOMENT_STEPS)
                nc.vector.scalar_tensor_tensor(out=minus_mean[Z], in0=mean[Z], scalar=-1.0,
                                               in1=rstd[Z], op0=ALU.mult,
                                               op1=ALU.mult).then_inc(minus_mean_done[Z], 1)
                nc.vector.tensor_tensor(x_var[:, par_tiles(k)], var[Z], rstd[Z][:, :], ALU.mult).then_inc(x_var_done, 1)
                yield
                dve.wait_ge(x_var_done, 3 * n - 2)
                nc.vector.tensor_tensor(x_var[:, par_tiles(k)], x_var[:, par_tiles(k)], rstd[Z][:, :], ALU.mult).then_inc(x_var_done, 1)
                yield
                dve.wait_ge(x_var_done, 3 * n - 1)
                nc.vector.tensor_scalar(x_var[:, par_tiles(k)], x_var[:, par_tiles(k)], EPS_OUT, None, ALU.add).then_inc(x_var_done, 1)

            def low_x(it, k):
                n = upto_chunk(it, k)
                c = half(k % 2)
                dve.wait_ge(xe_h_done, n)
                nc.vector.tensor_tensor(xe_l[:, c], C[:, :], xe_h[:, c].bitcast(F32), ALU.subtract).then_inc(xe_l_done, 1)

            def squares(it, k, t):
                n = upto_chunk(it, k)
                dve.wait_ge(gram_mm, (n - 1) * TILES + t + 1)
                if t == 0:
                    after(dve, hid_std_done, 2 * (n - 1))
                for e in range(EXPERTS):
                    i = t * EXPERTS + e
                    nc.vector.scalar_tensor_tensor(out=unused[:, tile(i % 8)], in0=O[0][:, tile(e)], scalar=1.0,
                                                   in1=xt[:, par_tile(k, t)], op0=ALU.mult, op1=ALU.mult,
                                                   accum_out=hid_var[:, i:i + 1]).then_inc(square_done, 1)
                    yield

            def split_std(it, k):
                n = upto_chunk(it, k)
                parts = std_parts[:, :].rearrange("p (t j e) -> p t j e", t=TILES, j=3)
                std = by_tile(hid_std[:, 0:TE])
                high = by_tile(std_h[:, :].bitcast(F32))
                dve.wait_ge(hid_std_done, 2 * n - 1)
                nc.vector.tensor_copy(std_h[:, :], hid_std[:, 0:TE]).then_inc(std_split, 1)
                dve.wait_ge(std_split, 3 * n - 2)
                nc.vector.tensor_copy(parts[:, :, 0:3:2, :],
                                      high.unsqueeze(2).to_broadcast([P, TILES, 2, EXPERTS])).then_inc(std_split, 1)
                nc.vector.tensor_tensor(parts[:, :, 1, :], std, high, ALU.subtract).then_inc(std_split, 1)

            def gates(it, k):
                n = upto_chunk(it, k)
                first = (n - 1) * GATE_STEPS
                done = [0]

                def previous():
                    dve.wait_ge(gate_step, first + done[0])

                def count(instruction):
                    instruction.then_inc(gate_step, 1)
                    done[0] += 1

                four = [P, TILES, EXPERTS, EXPERTS]
                dve.wait_ge(router_mm, n)
                dve.wait_ge(x_rstd_done, n)
                count(nc.vector.tensor_tensor(by_tile(logits[:, :]), by_tile(O[0][:, 0:TE]),
                                              over_experts(x_rstd[:, par_tiles(k)]), ALU.mult))
                yield
                previous()
                count(nc.vector.tensor_tensor(by_tile(logits[:, :]), by_tile(logits[:, :]),
                                              over_tiles(router_b[:, :], EXPERTS), ALU.add))
                yield
                previous()
                count(nc.vector.tensor_reduce(tile_sum[:, :], by_tile(logits[:, :]), AX.X, ALU.max))
                yield
                previous()
                count(nc.vector.tensor_tensor(by_tile(logits[:, :]), by_tile(logits[:, :]),
                                              over_experts(tile_sum[:, :]), ALU.subtract))
                yield
                dve.wait_ge(exps_done, n)
                count(nc.vector.tensor_reduce(tile_sum[:, :], by_tile(exps[:, :]), AX.X, ALU.add))
                yield
                previous()
                count(nc.vector.reciprocal(tile_rec[:, :], tile_sum[:, :]))
                yield
                previous()
                count(nc.vector.tensor_tensor(by_tile(prob[:, :]), by_tile(exps[:, :]),
                                              over_experts(tile_rec[:, :]), ALU.mult))
                yield
                previous()
                other = by_tile(prob[:, :]).unsqueeze(2).to_broadcast(four)
                own = by_tile(prob[:, :]).unsqueeze(3).to_broadcast(four)
                pairs = "p (t e j) -> p t e j"
                for out_, op in ((not_less, ALU.is_ge), (greater, ALU.is_gt)):
                    count(nc.vector.tensor_tensor(out_[:, :].rearrange(pairs, t=TILES, e=EXPERTS), other, own, op))
                yield
                previous()
                for out_, c in ((not_less, 0), (greater, TE)):
                    count(nc.vector.tensor_tensor(by_tile(out_[:, :]), by_tile(out_[:, :]),
                                                  over_tiles(masks[:, c:c + TE], TE), ALU.mult))
                yield
                previous()
                count(nc.vector.tensor_tensor(not_less[:, :], not_less[:, :], greater[:, :], ALU.add))
                yield
                previous()
                count(nc.vector.tensor_reduce(rank[:, :], not_less[:, :].rearrange("p (i j) -> p i j", j=EXPERTS),
                                              AX.X, ALU.add))
                yield
                previous()
                count(nc.vector.scalar_tensor_tensor(out=top2[:, :], in0=rank[:, :], scalar=2.0, in1=prob[:, :],
                                                     op0=ALU.is_lt, op1=ALU.mult))
                yield
                previous()
                count(nc.vector.tensor_reduce(tile_sum[:, :], by_tile(top2[:, :]), AX.X, ALU.add))
                yield
                previous()
                count(nc.vector.tensor_scalar(tile_sum[:, :], tile_sum[:, :], EPS_GATE, None, ALU.add))
                yield
                previous()
                count(nc.vector.reciprocal(tile_rec[:, :], tile_sum[:, :]))
                yield
                previous()
                count(nc.vector.tensor_tensor(by_tile(top2[:, :]), by_tile(top2[:, :]),
                                              over_experts(tile_rec[:, :]), ALU.mult))
                yield
                previous()
                dve.wait_ge(hid_std_done, 2 * n)
                count(nc.vector.tensor_tensor(gate[:, k % 2 * TE:(k % 2 + 1) * TE], top2[:, :],
                                              hid_std[:, TE:2 * TE], ALU.mult))
                assert done[0] == GATE_STEPS

            def mix_tile(it, k, t):
                n = upto_chunk(it, k)
                first = ((n - 1) * TILES + t) * EXPERTS
                dve.wait_ge(expert_out_mm, (n - 1) * TILES + t + 1)
                dve.wait_ge(gate_step, n * GATE_STEPS)
                for e in range(EXPERTS):
                    c = k % 2 * TE + t * EXPERTS + e
                    o = mix[:, par_tile(k, t)]
                    if e == 0:
                        nc.vector.tensor_scalar(o, MIXED[t % 2][:, tile(e)], gate[:, c:c + 1], None,
                                                ALU.mult).then_inc(mix_done, 1)
                    else:
                        dve.wait_ge(mix_done, first + e)
                        nc.vector.scalar_tensor_tensor(out=o, in0=MIXED[t % 2][:, tile(e)], scalar=gate[:, c:c + 1],
                                                       in1=o, op0=ALU.mult, op1=ALU.add).then_inc(mix_done, 1)
                    yield

            def stats_mix(it, k):
                dve.wait_ge(mix_done, upto_chunk(it, k) * TE)
                yield from statistics(MIX, it, k, mix[:, half(k % 2)])

            def stats_sum(it, k):
                dve.wait_ge(sum_done, upto_chunk(it, k))
                yield from statistics(SUM, it, k, mix[:, half(k % 2)])

            def negate_mean(which, it, k):
                dve.wait_ge(rstd_done[which], upto_chunk(it, k))
                dve.wait_ge(moments_step[which], upto_chunk(it, k) * MOMENT_STEPS)
                nc.vector.scalar_tensor_tensor(out=minus_mean[which], in0=mean[which], scalar=-1.0, in1=rstd[which],
                                               op0=ALU.mult, op1=ALU.mult).then_inc(minus_mean_done[which], 1)

            def weave(*sequences):
                ended = object()
                left = list(sequences)
                while left:
                    left = [sequence for sequence in left if next(sequence, ended) is not ended]

            def step(it, k, attends, feeds, ends, projects):
                if projects:
                    kvq_sums(it, projected(it, k), 0)
                if feeds:
                    finish(0, it, k - 1, 0)
                if ends:
                    split_y(1, it, k - 2, 1)
                if k == 5 and not projects:
                    prepare_bias()
                if projects:
                    kvq_sums(it, projected(it, k), 1)
                if k == 5 and projects:
                    install_bias_f(it + 1)
                if feeds:
                    finish(0, it, k - 1, 1)
                if k == 4 and not projects:
                    prepare_w1()
                if attends:
                    attend(it, k, 0)
                    attend(it, k, 1)
                if ends:
                    add_eps(1, it, k - 2)
                if k == 5 and not projects:
                    add_input(0, 0)
                    weave(stats_z(0, 0))
                if k == 5 and not projects:
                    prepare_gram()
                if k == 2 or (k == 6 and projects):
                    if k == 2:
                        dve.wait_ge(wrest_loaded, 16 * (LAYERS - 1))
                        dve.wait_ge(pad_set, 2)
                    install_qkv(layer(it, k - 3) + 2, it, k - 3)
                if attends:
                    split_y(0, it, k, 0)
                if ends:
                    split_rs(1, it, k - 2)
                if k == 5 and not projects:
                    weave(scale_x(0, 0))
                if attends:
                    split_y(0, it, k, 1)
                if k == 3 and projects:
                    install_wo(it + 1, it, k)
                if projects:
                    kvq_q(it, projected(it, k), 0)
                if k == 3 and projects:
                    install_bias_o(it + 1)
                if ends:
                    finish(1, it, k - 2, 0)
                    finish(1, it, k - 2, 1)
                if k == 5 and not projects:
                    low_x(0, 0)
                if projects:
                    kvq_q(it, projected(it, k), 1)
                if attends:
                    add_eps(0, it, k)
                if k == 2 or (k == 6 and projects):
                    install_bias_qk(layer(it, k - 3) + 2)
                if feeds:
                    split_y(1, it, k - 1, 0)
                if attends:
                    split_rs(0, it, k)
                if k == 4 and projects:
                    install_wf(it + 1, it, k - 1)

            dve.wait_ge(wfirst_loaded, 16)
            raw = wraw[:, 0:QKV]
            nc.vector.tensor_copy(wqkv_h[:, :], raw).then_inc(wqkv_high, 1)
            dve.wait_ge(wqkv_high, 1)
            nc.vector.tensor_tensor(wqkv_l[:, :], raw, wqkv_h[:, :].bitcast(F32),
                                    ALU.subtract).then_inc(wqkv_set, 1)

            def split_first(c):
                dve.wait_ge(x_loaded[c], 16)
                after(dve, kvq_mm, 3 * (c - 3))
                nc.vector.tensor_copy(xr_h[:, ring(c // 2, c % 2)],
                                      x[:, c * CH:(c + 1) * CH]).then_inc(xh_done[1], 1)

            split_first(0)
            split_first(1)
            install_wo(0, 0, -1)
            install_wf(0, 0, -1)
            install_bias_qk(0)
            install_bias_o(0)
            install_bias_f(0)
            for c in range(4):
                split_first(c + 2)
                kvq_sums(0, c // 2 - 4, c % 2)
                kvq_q(0, c // 2 - 4, c % 2)
            split_first(6)
            split_first(7)
            run(nc.vector, step)



            def step(it, k, enters, routes, mixes, ends):
                none = iter(())
                gating = gates(it, k) if routes else none
                if enters:
                    add_input(it, k + 1)
                weave(squares(it, k, 0) if routes else none, stats_mix(it, k - 2) if ends else none)
                weave(squares(it, k, 1) if routes else none, stats_z(it, k + 1) if enters else none)
                if ends:
                    negate_mean(MIX, it, k - 2)
                weave(squares(it, k, 2) if routes else none, scale_x(it, k + 1) if enters else none)
                if routes:
                    weave(squares(it, k, 3))
                weave(itertools.islice(gating, 7))
                if routes:
                    split_std(it, k)
                if enters:
                    low_x(it, k + 1)
                weave(mix_tile(it, k - 1, 0) if mixes else none, itertools.islice(gating, 4))
                summing = stats_sum(it, k - 2) if ends else none
                weave(mix_tile(it, k - 1, 1) if mixes else none, itertools.islice(gating, 3), summing)
                weave(mix_tile(it, k - 1, 2) if mixes else none, gating)
                weave(mix_tile(it, k - 1, 3) if mixes else none)
                if ends:
                    negate_mean(SUM, it, k - 2)

            run_moe(nc.vector, step)

        @block.gpsimd
        def _(pool):
            nc.gpsimd.memset(moe_eps[:, :], EPS_OUT).then_inc(moe_eps_set, 1)
            nc.gpsimd.memset(mhalf[:, :], -0.5).then_inc(mhalf_set, 1)
            nc.gpsimd.memset(wraw[:, LAYERS * WCOLS:], 0.0).then_inc(pad_set, 1)
            nc.gpsimd.memset(par[:, LAYERS * NPAR:], 0.0).then_inc(pad_set, 1)
            pool.wait_ge(mhalf_set, 1)

            def residual(which, it, k, h):
                n = upto(it, k, h)
                pool.wait_ge(gelu_done[which], n)
                if which == 0:
                    pool.wait_ge(xh_done[1], n)
                else:
                    pool.wait_ge(xf_done[0], n)
                inp = (x[:, chunk(k, h)], x1[:, ring(k, h)])[which]
                nc.gpsimd.tensor_tensor(y[which][:, half(h)], y[which][:, half(h)], inp,
                                        ALU.add).then_inc(y_done[which], 1)

            def rsqrt(which, it, k):
                pool.wait_ge(ve_done[which], units_upto(it, k))
                nc.gpsimd.tensor_tensor(rs[which][:, :], ve[which][:, :], mhalf[:, :],
                                        ALU.pow).then_inc(rs_done[which], 1)

            def low(which, it, k, h):
                n = splits_upto(which, it, k, h)
                full, high, lo = ((x1[:, ring(k, h)], x1_h[:, ring(k, h)], x1_l[:, ring(k, h)]),
                                  (x[:, chunk(k, h)], xr_h[:, ring(k, h)], xr_l[:, ring(k, h)]))[which]
                pool.wait_ge(xh_done[which], n)
                nc.gpsimd.tensor_tensor(lo, full, high.bitcast(F32), ALU.subtract).then_inc(xl_done[which], 1)

            def to_minus_half(which, it, k):
                pool.wait_ge(var_eps_done[which], upto_chunk(it, k))
                nc.gpsimd.tensor_tensor(rstd[which][:, :], var_eps[which][:, :], mhalf[:, 0:TILES],
                                        ALU.pow).then_inc(rstd_done[which], 1)

            def x_to_minus_half(it, k):
                pool.wait_ge(x_var_done, 3 * upto_chunk(it, k))
                nc.gpsimd.tensor_tensor(x_rstd[:, par_tiles(k)], x_var[:, par_tiles(k)], mhalf[:, 0:TILES], ALU.pow).then_inc(x_rstd_done, 1)

            def scale_and_add(it, k):
                n = upto_chunk(it, k)
                o = mix[:, half(k % 2)]
                pool.wait_ge(mix_normed, n * TILES)
                nc.gpsimd.tensor_tensor(by_tile(o), by_tile(o), over_tiles(on_g, P), ALU.mult).then_inc(mix_scaled, 1)
                pool.wait_ge(mix_scaled, n)
                pool.wait_ge(xb_done, n)
                nc.gpsimd.tensor_tensor(o, o, xb[:, half(k % 2)], ALU.add).then_inc(sum_done, 1)

            def add_on_b(it, k):
                n = upto_chunk(it, k)
                pool.wait_ge(moe_loaded, 16 * 6)
                pool.wait_ge(xt_done, n * TILES)
                after(pool, sum_done, n - 2)
                nc.gpsimd.tensor_tensor(by_tile(xb[:, half(k % 2)]), by_tile(xt[:, half(k % 2)]),
                                        over_tiles(on_b, P), ALU.add).then_inc(xb_done, 1)

            def step(it, k, attends, feeds, ends, projects):
                if ends:
                    residual(1, it, k - 2, 1)
                if feeds:
                    low(0, it, k - 1, 0)
                    low(0, it, k - 1, 1)
                if ends:
                    rsqrt(1, it, k - 2)
                if k == 5 and not projects:
                    to_minus_half(0, 0, 0)
                    x_to_minus_half(0, 0)
                if attends:
                    residual(0, it, k, 0)
                    residual(0, it, k, 1)
                if feeds:
                    residual(1, it, k - 1, 0)
                if ends and splits(1, it, k - 2):
                    low(1, it, k - 2, 0)
                    low(1, it, k - 2, 1)
                if attends:
                    rsqrt(0, it, k)

            for c in range(8):
                after(pool, kvq_mm, 3 * (c - 3))
                low(1, 0, c // 2 - 4, c % 2)
            run(nc.gpsimd, step)


            def step(it, k, enters, routes, mixes, ends):
                if ends:
                    to_minus_half(1, it, k - 2)
                if mixes:
                    add_on_b(it, k - 1)
                if enters:
                    to_minus_half(0, it, k + 1)
                    x_to_minus_half(it, k + 1)
                if ends:
                    scale_and_add(it, k - 2)
                if ends:
                    to_minus_half(2, it, k - 2)

            run_moe(nc.gpsimd, step)


def kernel(**inputs):
    import numpy as np
    import concourse.bacc as bacc
    from concourse.bass_utils import run_bass_kernel_spmd

    a = {k[3:]: np.asarray(v) for k, v in inputs.items()}
    rows = lambda w: w.transpose(1, 0, 2)
    x = np.ascontiguousarray(a["attn_x"].reshape(-1, P).T)
    wf2 = a["attn_Wf2"].reshape(LAYERS, FB, P, P).transpose(2, 0, 1, 3).reshape(P, LAYERS, FB * P)
    w = np.concatenate([rows(a["attn_Wq"]), rows(a["attn_Wk"]), rows(a["attn_Wv"]), rows(a["attn_Wo"]),
                        rows(a["attn_Wf1"]), wf2], axis=2).reshape(P, -1)
    cols = [a["attn_" + n].T[:, :, None] for n in ("bq", "bk", "bv", "bo", "ln1_s", "ln1_b", "ln2_s", "ln2_b", "bf2")]
    cols.append(a["attn_bf1"].reshape(LAYERS, FB, P).transpose(2, 0, 1))
    par = np.concatenate(cols, axis=2).reshape(P, -1)
    sel = np.zeros((P, 2 * TILES, P), np.float32)
    for t in range(2 * TILES):
        sel[t, t] = sel[LOW + t, t] = 1.0
    before = np.tril(np.ones((EXPERTS, EXPERTS)), -1)
    row_mask = np.zeros((P, 2, EXPERTS))
    for j in range(3):
        for e in range(EXPERTS):
            row_mask[j * EXPERTS + e, j // 2, e] = 1.0
    const = np.concatenate([np.eye(P), np.eye(P) - 1.0 / P, sel.reshape(P, -1),
                            np.broadcast_to(before.reshape(1, -1), (P, TE)),
                            np.broadcast_to(before.T.reshape(1, -1), (P, TE)),
                            row_mask.reshape(P, -1)], axis=1).astype(np.float32)
    w1 = a["ffn_w1"].transpose(1, 0, 2).reshape(P, EW)
    w2 = a["ffn_w2"].reshape(HB, P, P).transpose(1, 0, 2).reshape(P, EW)
    moe = np.concatenate([a["ffn_rn_g"][:, None], a["ffn_rn_b"][:, None], a["ffn_router_w"].T], axis=1)
    row = np.concatenate([a["ffn_ln_g"].ravel(), a["ffn_ln_b"].ravel(), a["ffn_on_g"], a["ffn_on_b"]])[None]
    arrays = {"x": x, "w": w, "par": par, "const": const, "w1": w1, "w2": w2, "moe": moe, "row": row}
    arrays = {k: np.ascontiguousarray(v) for k, v in arrays.items()}
    nc = bacc.Bacc("TRN2", target_bir_lowering=False, num_devices=1)
    args = [nc.dram_tensor(k + "_dram", v.shape, F32, kind="ExternalInput").ap() for k, v in arrays.items()]
    out = nc.dram_tensor("out_dram", (x.shape[1], P), F32, kind="ExternalOutput").ap()
    build(nc, *args, out.rearrange("(c p) d -> p c d", p=P))
    r = run_bass_kernel_spmd(nc, [{k + "_dram": v for k, v in arrays.items()}], core_ids=[0])
    return r.results[0]["out_dram"].reshape(a["attn_x"].shape)
```
